# Optimizing a Trainium2 kernel written in Bass

```python
import numpy as np
import jax
import jax.numpy as jnp

def _softmax(x, axis=-1):
    return jax.nn.softmax(x, axis=axis)

def _gelu(x):
    return jax.nn.gelu(x, approximate=True)

def _silu(x):
    return jax.nn.silu(x)

def _sigmoid(x):
    return jax.nn.sigmoid(x)

def _layernorm(x, axis=-1, eps=1e-05):
    m = jnp.mean(x, axis=axis, keepdims=True)
    v = jnp.var(x, axis=axis, keepdims=True)
    return (x - m) / jnp.sqrt(v + eps)

def _scatter_add(tgt, idx, src, axis=0):
    return tgt.at[idx].add(src)

def _segment_sum(src, seg, n):
    return jax.ops.segment_sum(src, seg, n)
kernel_name = 'mk_dlrm_tower_d1_rec_r8_325c94'

def setup_inputs(seed: int=0):
    np.random.seed(seed)
    _w = jnp.asarray

    def _rec_inputs():
        import jax
        import jax.numpy as jnp
        _tk = jax.random.key(seed)
        dense_ctx = jax.random.normal(jax.random.fold_in(_tk, 190), (2048, 16), jnp.float32)
        ids = jnp.stack([jax.random.randint(jax.random.fold_in(_tk, 200 + f), (2048,), 0, v, jnp.int32) for f, v in enumerate([12500, 1250, 1250, 125000, 1250, 12500, 125000, 1000, 1000, 125000, 12500, 1250, 12500, 1250, 1000, 1250, 1250, 1250, 1250, 1250, 1000, 1000, 1250, 1000, 1250, 12500, 12500, 1250, 1250, 12500, 1250, 1000, 1000, 1000, 1000, 1250, 1250, 1000, 1000, 1250])], axis=1)
        tbl_0 = 0.05 * jax.random.normal(jax.random.fold_in(_tk, 500 + 0), (12500, 64), jnp.float32)
        tbl_1 = 0.05 * jax.random.normal(jax.random.fold_in(_tk, 500 + 1), (1250, 64), jnp.float32)
        tbl_2 = 0.05 * jax.random.normal(jax.random.fold_in(_tk, 500 + 2), (1250, 64), jnp.float32)
        tbl_3 = 0.05 * jax.random.normal(jax.random.fold_in(_tk, 500 + 3), (125000, 64), jnp.float32)
        tbl_4 = 0.05 * jax.random.normal(jax.random.fold_in(_tk, 500 + 4), (1250, 64), jnp.float32)
        tbl_5 = 0.05 * jax.random.normal(jax.random.fold_in(_tk, 500 + 5), (12500, 64), jnp.float32)
        tbl_6 = 0.05 * jax.random.normal(jax.random.fold_in(_tk, 500 + 6), (125000, 64), jnp.float32)
        tbl_7 = 0.05 * jax.random.normal(jax.random.fold_in(_tk, 500 + 7), (1000, 64), jnp.float32)
        tbl_8 = 0.05 * jax.random.normal(jax.random.fold_in(_tk, 500 + 8), (1000, 64), jnp.float32)
        tbl_9 = 0.05 * jax.random.normal(jax.random.fold_in(_tk, 500 + 9), (125000, 64), jnp.float32)
        tbl_10 = 0.05 * jax.random.normal(jax.random.fold_in(_tk, 500 + 10), (12500, 64), jnp.float32)
        tbl_11 = 0.05 * jax.random.normal(jax.random.fold_in(_tk, 500 + 11), (1250, 64), jnp.float32)
        tbl_12 = 0.05 * jax.random.normal(jax.random.fold_in(_tk, 500 + 12), (12500, 64), jnp.float32)
        tbl_13 = 0.05 * jax.random.normal(jax.random.fold_in(_tk, 500 + 13), (1250, 64), jnp.float32)
        tbl_14 = 0.05 * jax.random.normal(jax.random.fold_in(_tk, 500 + 14), (1000, 64), jnp.float32)
        tbl_15 = 0.05 * jax.random.normal(jax.random.fold_in(_tk, 500 + 15), (1250, 64), jnp.float32)
        tbl_16 = 0.05 * jax.random.normal(jax.random.fold_in(_tk, 500 + 16), (1250, 64), jnp.float32)
        tbl_17 = 0.05 * jax.random.normal(jax.random.fold_in(_tk, 500 + 17), (1250, 64), jnp.float32)
        tbl_18 = 0.05 * jax.random.normal(jax.random.fold_in(_tk, 500 + 18), (1250, 64), jnp.float32)
        tbl_19 = 0.05 * jax.random.normal(jax.random.fold_in(_tk, 500 + 19), (1250, 64), jnp.float32)
        tbl_20 = 0.05 * jax.random.normal(jax.random.fold_in(_tk, 500 + 20), (1000, 64), jnp.float32)
        tbl_21 = 0.05 * jax.random.normal(jax.random.fold_in(_tk, 500 + 21), (1000, 64), jnp.float32)
        tbl_22 = 0.05 * jax.random.normal(jax.random.fold_in(_tk, 500 + 22), (1250, 64), jnp.float32)
        tbl_23 = 0.05 * jax.random.normal(jax.random.fold_in(_tk, 500 + 23), (1000, 64), jnp.float32)
        tbl_24 = 0.05 * jax.random.normal(jax.random.fold_in(_tk, 500 + 24), (1250, 64), jnp.float32)
        tbl_25 = 0.05 * jax.random.normal(jax.random.fold_in(_tk, 500 + 25), (12500, 64), jnp.float32)
        tbl_26 = 0.05 * jax.random.normal(jax.random.fold_in(_tk, 500 + 26), (12500, 64), jnp.float32)
        tbl_27 = 0.05 * jax.random.normal(jax.random.fold_in(_tk, 500 + 27), (1250, 64), jnp.float32)
        tbl_28 = 0.05 * jax.random.normal(jax.random.fold_in(_tk, 500 + 28), (1250, 64), jnp.float32)
        tbl_29 = 0.05 * jax.random.normal(jax.random.fold_in(_tk, 500 + 29), (12500, 64), jnp.float32)
        tbl_30 = 0.05 * jax.random.normal(jax.random.fold_in(_tk, 500 + 30), (1250, 64), jnp.float32)
        tbl_31 = 0.05 * jax.random.normal(jax.random.fold_in(_tk, 500 + 31), (1000, 64), jnp.float32)
        tbl_32 = 0.05 * jax.random.normal(jax.random.fold_in(_tk, 500 + 32), (1000, 64), jnp.float32)
        tbl_33 = 0.05 * jax.random.normal(jax.random.fold_in(_tk, 500 + 33), (1000, 64), jnp.float32)
        tbl_34 = 0.05 * jax.random.normal(jax.random.fold_in(_tk, 500 + 34), (1000, 64), jnp.float32)
        tbl_35 = 0.05 * jax.random.normal(jax.random.fold_in(_tk, 500 + 35), (1250, 64), jnp.float32)
        tbl_36 = 0.05 * jax.random.normal(jax.random.fold_in(_tk, 500 + 36), (1250, 64), jnp.float32)
        tbl_37 = 0.05 * jax.random.normal(jax.random.fold_in(_tk, 500 + 37), (1000, 64), jnp.float32)
        tbl_38 = 0.05 * jax.random.normal(jax.random.fold_in(_tk, 500 + 38), (1000, 64), jnp.float32)
        tbl_39 = 0.05 * jax.random.normal(jax.random.fold_in(_tk, 500 + 39), (1250, 64), jnp.float32)
        _rk = jax.random.fold_in(_tk, 7)
        W_top1 = 0.0354441 * jax.random.normal(jax.random.fold_in(_tk, 801), (796, 512), jnp.float32)
        W_top2 = 0.0441942 * jax.random.normal(jax.random.fold_in(_tk, 802), (512, 256), jnp.float32)
        W_top3 = 0.0625 * jax.random.normal(jax.random.fold_in(_tk, 803), (256, 1), jnp.float32)
        b_top1 = jnp.zeros((512,), jnp.float32)
        b_top2 = jnp.zeros((256,), jnp.float32)
        return (dense_ctx, ids, tbl_0, tbl_1, tbl_2, tbl_3, tbl_4, tbl_5, tbl_6, tbl_7, tbl_8, tbl_9, tbl_10, tbl_11, tbl_12, tbl_13, tbl_14, tbl_15, tbl_16, tbl_17, tbl_18, tbl_19, tbl_20, tbl_21, tbl_22, tbl_23, tbl_24, tbl_25, tbl_26, tbl_27, tbl_28, tbl_29, tbl_30, tbl_31, tbl_32, tbl_33, tbl_34, tbl_35, tbl_36, tbl_37, tbl_38, tbl_39, W_top1, b_top1, W_top2, b_top2, W_top3)
    dense_ctx, ids, tbl_0, tbl_1, tbl_2, tbl_3, tbl_4, tbl_5, tbl_6, tbl_7, tbl_8, tbl_9, tbl_10, tbl_11, tbl_12, tbl_13, tbl_14, tbl_15, tbl_16, tbl_17, tbl_18, tbl_19, tbl_20, tbl_21, tbl_22, tbl_23, tbl_24, tbl_25, tbl_26, tbl_27, tbl_28, tbl_29, tbl_30, tbl_31, tbl_32, tbl_33, tbl_34, tbl_35, tbl_36, tbl_37, tbl_38, tbl_39, W_top1, b_top1, W_top2, b_top2, W_top3 = _rec_inputs()

    def _L0_rec_setup():
        import jax, jax.numpy as jnp
        import numpy as np

        def _pair_indices(num_fields):
            i_idx, j_idx = np.triu_indices(num_fields, k=1)
            return (jnp.asarray(i_idx), jnp.asarray(j_idx))
        key = jax.random.key(seed)
        k1, k2 = jax.random.split(key)
        B, F, D = (256, 40, 64)
        P = F * (F - 1) // 2
        x = jax.random.normal(k1, (B, F, D), dtype=jnp.float32)
        W = jax.random.normal(k2, (P, D, D), dtype=jnp.float32) * (1.0 / np.sqrt(D))
        return {'x': x, 'W': W}
    _L0_rec_all = _L0_rec_setup()
    _L0_rec_in = {k: v for k, v in _L0_rec_all.items() if k in ('W',)}
    del _L0_rec_all
    return {'dense_ctx': dense_ctx, 'ids': ids, 'tbl_0': tbl_0, 'tbl_1': tbl_1, 'tbl_2': tbl_2, 'tbl_3': tbl_3, 'tbl_4': tbl_4, 'tbl_5': tbl_5, 'tbl_6': tbl_6, 'tbl_7': tbl_7, 'tbl_8': tbl_8, 'tbl_9': tbl_9, 'tbl_10': tbl_10, 'tbl_11': tbl_11, 'tbl_12': tbl_12, 'tbl_13': tbl_13, 'tbl_14': tbl_14, 'tbl_15': tbl_15, 'tbl_16': tbl_16, 'tbl_17': tbl_17, 'tbl_18': tbl_18, 'tbl_19': tbl_19, 'tbl_20': tbl_20, 'tbl_21': tbl_21, 'tbl_22': tbl_22, 'tbl_23': tbl_23, 'tbl_24': tbl_24, 'tbl_25': tbl_25, 'tbl_26': tbl_26, 'tbl_27': tbl_27, 'tbl_28': tbl_28, 'tbl_29': tbl_29, 'tbl_30': tbl_30, 'tbl_31': tbl_31, 'tbl_32': tbl_32, 'tbl_33': tbl_33, 'tbl_34': tbl_34, 'tbl_35': tbl_35, 'tbl_36': tbl_36, 'tbl_37': tbl_37, 'tbl_38': tbl_38, 'tbl_39': tbl_39, 'W_top1': W_top1, 'b_top1': b_top1, 'W_top2': W_top2, 'b_top2': b_top2, 'W_top3': W_top3, 'L0_rec_W': _L0_rec_in['W']}

def reference(dense_ctx, ids, tbl_0, tbl_1, tbl_2, tbl_3, tbl_4, tbl_5, tbl_6, tbl_7, tbl_8, tbl_9, tbl_10, tbl_11, tbl_12, tbl_13, tbl_14, tbl_15, tbl_16, tbl_17, tbl_18, tbl_19, tbl_20, tbl_21, tbl_22, tbl_23, tbl_24, tbl_25, tbl_26, tbl_27, tbl_28, tbl_29, tbl_30, tbl_31, tbl_32, tbl_33, tbl_34, tbl_35, tbl_36, tbl_37, tbl_38, tbl_39, W_top1, b_top1, W_top2, b_top2, W_top3, L0_rec_W):
    import jax
    import jax.numpy as jnp

    def _L0_rec_ref(x, W):
        import jax, jax.numpy as jnp
        import numpy as np

        def _pair_indices(num_fields):
            i_idx, j_idx = np.triu_indices(num_fields, k=1)
            return (jnp.asarray(i_idx), jnp.asarray(j_idx))
        B, F, D = x.shape
        i_idx, j_idx = _pair_indices(F)
        vi = x[:, i_idx, :]
        vj = x[:, j_idx, :]
        viW = jnp.einsum('bpd,pde->bpe', vi, W)
        out = jnp.einsum('bpe,bpe->bp', viW, vj)
        return out
    e = jnp.stack([tbl_0[ids[:, 0]], tbl_1[ids[:, 1]], tbl_2[ids[:, 2]], tbl_3[ids[:, 3]], tbl_4[ids[:, 4]], tbl_5[ids[:, 5]], tbl_6[ids[:, 6]], tbl_7[ids[:, 7]], tbl_8[ids[:, 8]], tbl_9[ids[:, 9]], tbl_10[ids[:, 10]], tbl_11[ids[:, 11]], tbl_12[ids[:, 12]], tbl_13[ids[:, 13]], tbl_14[ids[:, 14]], tbl_15[ids[:, 15]], tbl_16[ids[:, 16]], tbl_17[ids[:, 17]], tbl_18[ids[:, 18]], tbl_19[ids[:, 19]], tbl_20[ids[:, 20]], tbl_21[ids[:, 21]], tbl_22[ids[:, 22]], tbl_23[ids[:, 23]], tbl_24[ids[:, 24]], tbl_25[ids[:, 25]], tbl_26[ids[:, 26]], tbl_27[ids[:, 27]], tbl_28[ids[:, 28]], tbl_29[ids[:, 29]], tbl_30[ids[:, 30]], tbl_31[ids[:, 31]], tbl_32[ids[:, 32]], tbl_33[ids[:, 33]], tbl_34[ids[:, 34]], tbl_35[ids[:, 35]], tbl_36[ids[:, 36]], tbl_37[ids[:, 37]], tbl_38[ids[:, 38]], tbl_39[ids[:, 39]]], axis=1)
    z = _L0_rec_ref(e, L0_rec_W)
    z = z.reshape(z.shape[0], -1)
    h = jnp.concatenate([z, dense_ctx], axis=1)
    h = jnp.maximum(h @ W_top1 + b_top1, 0.0)
    h = jnp.maximum(h @ W_top2 + b_top2, 0.0)
    y = h @ W_top3
    return y

_drawn_inputs = setup_inputs


def setup_inputs(seed=0):
    import zlib

    import numpy as np

    out = dict(_drawn_inputs(seed))
    spreads = {'b_top1': (0.0, 0.1), 'b_top2': (0.0, 0.1)}
    factors = {}
    for name, (base, spread) in spreads.items():
        noise = np.random.default_rng([zlib.crc32(name.encode()), seed]).standard_normal(out[name].shape)
        drawn = base * np.exp(spread * noise) if base else spread * noise
        out[name] = jnp.asarray(drawn.astype(out[name].dtype))
    for name, factor in factors.items():
        out[name] = (out[name] * factor).astype(out[name].dtype)
    return out
```

```python
import concourse.bass as bass
import concourse.mybir as mybir
import numpy as np
from contextlib import ExitStack

B, F, D, DENSE = 2048, 40, 64, 16
N1, N2 = 512, 256
P128 = 128
GROUPS = 2
GB = B // GROUPS
HALF = 512
CHUNKS = GB // HALF
TILES = GB // P128
PAIRS = F // 2


def block_list():
    out = []
    for k in reversed(range(PAIRS)):
        for i in (2 * k + 1, 2 * k):
            out += [(i, jp) for jp in range(PAIRS - 1, k, -1)]
        out.append((2 * k, k))
    return out


BLOCKS = block_list()
NB = len(BLOCKS)
QUADS = NB // 4
ZQ = 16
ZT = -(-QUADS // ZQ)
DENSE_ROW = 16
W_COLS = 2 * D
LOAD_BLOCKS = 8
FIELDS = F - 1
START = {}
for _n, (_i, _jp) in enumerate(BLOCKS):
    START.setdefault(_i, _n)
COUNT = {i: sum(1 for a, _ in BLOCKS if a == i) for i in START}


def mlp_slot(g, what, k):
    quad = g * QUADS + QUADS - 3 + {"w1": 0, "h1": 1, "h2": 2}[what]
    return 4 * (quad % (P_SLOTS // 4)) + k


def z_place(n, half):
    q, strip = n // 4, n % 4
    return 32 * strip + 2 * (q % ZQ) + half, q // ZQ


U_SLOTS, P_SLOTS, WF_SLOTS, WQ_SLOTS = 3, 12, 2, 3
MLP_STEPS = N1 // P128 + N2 // P128 + 1


RED_LAG = 6
DVE_QUADS = 22
DIRECT = 10


def tr_at(g, r):
    if r < 2:
        return g * NB - 6 + 2 * r
    if g == 0 and r < DIRECT:
        return r * r - r
    return g * NB + max((r - 1) ** 2, r * r - r - 4)


def mlp_at(g, m):
    return g * NB + NB + (-0.55 + 0.001 * m if m < 4 else (0.2, 1.2, 3.2)[m - 4])


def pe_order():
    steps = []
    for g in range(GROUPS):
        for r in range(PAIRS):
            steps.append((tr_at(g, r) - 0.5, ("tr", g, r)))
        for n in range(NB):
            steps.append((g * NB + n, ("main", g, n)))
        for q in range(QUADS):
            at = g * NB + 4 * q + RED_LAG + 0.2
            steps.append((min(at, g * NB + NB - 0.6), ("red", g, q)))
        steps.append((g * NB + NB - 0.601, ("early", g, 0)))
        for m in range(MLP_STEPS):
            steps.append((mlp_at(g, m), ("mlp", g, m)))
    return [s for _, s in sorted(steps, key=lambda x: x[0])]


PE_STEPS = pe_order()
U_USES = [("mlp",) + s[1:] if s[0] == "early" else s for s in PE_STEPS if s[0] != "red" and s[::2] != ("mlp", 0)]
U_AT = {s: k for k, s in enumerate(U_USES)}


def field_seq(g, f):
    return g * FIELDS + (FIELDS - 1 - f)


def hi_key(g, f):
    if f >= FIELDS - 2 and (g or f == FIELDS - 1):
        return g * NB - 0.57 + 0.001 * (FIELDS - 1 - f)
    if g and START[f + 1] == 4:
        return g * NB + 3.45
    return g * NB + START[f + 1] + min(0.5 * COUNT[f + 1], 3.0) + 0.1


def act_order():
    steps = []
    for g in range(GROUPS):
        for r in range(PAIRS):
            steps.append((tr_at(g, r) - 0.4, ("v", g, r)))
        for f in range(FIELDS):
            steps.append((hi_key(g, f), ("hi", g, f)))
        for q in range(QUADS):
            first = g == 0 and q < WQ_SLOTS
            steps.append((-20 + q if first else g * NB + 4 * q - 8, ("wh", g, q)))
        for t in range(ZT):
            q = min(ZQ * (t + 1), QUADS) - 1
            steps.append((min(g * NB + 4 * q + RED_LAG + 0.5, g * NB + NB - 0.58), ("z", g, t)))
        for m in range(MLP_STEPS):
            steps.append((mlp_at(g, m) + (0, 0, 0, 0, 0.3, 2.0, 0.3)[m], ("mlp", g, m)))
    return [s for _, s in sorted(steps, key=lambda x: x[0])]


def dve_order():
    steps = []
    for g in range(GROUPS):
        for n in range(NB):
            steps.append((g * NB + n, ("mul", g, n)))
        for q in range(DVE_QUADS if g == 0 else 0):
            steps.append((-19.5 + q if q < WQ_SLOTS else 4 * q - 7.5, ("wl", g, q)))
        for f in range(FIELDS):
            steps.append((max(hi_key(g, f) + 0.05, g * NB - 0.01) - 0.00001 * f, ("lo", g, f)))
    return [s for _, s in sorted(steps, key=lambda x: x[0])]


def sp_order():
    steps = []
    for g in range(GROUPS):
        for r in range(0 if g else DIRECT, PAIRS):
            before = tr_at(g, r - 1) if r else g * NB - 8
            steps.append((max(before + 0.3, tr_at(g, r) - 8), ("nat", g, r)))
        for f in range(FIELDS):
            if f >= FIELDS - 2:
                at = tr_at(g, PAIRS - 1 - f // 2) + 0.7 - 0.001 * f
            else:
                at = max(hi_key(g, f + 2) + 0.07, g * NB + 0.001, tr_at(g, PAIRS - 1 - f // 2) - 0.3)
            steps.append((at - 0.00001 * f, ("dup", g, f)))
        for c in range(NB // LOAD_BLOCKS):
            at = g * NB + LOAD_BLOCKS * c - 19
            steps.append((min(at, -18) if g == 0 and c < 2 else at, ("w", g, c)))
        steps.append((g * NB + NB - 5.5, ("w1", g, 0)))
    return [s for _, s in sorted(steps, key=lambda x: x[0])]


NEAR, FAR, RAMP, SLOPE = 1.5, 2.5, 8, 0.1
PACE, START_PACE = 3.5, 110


def pool_order():
    total = GROUPS * PAIRS * TILES * 2
    steps, done = [], 0
    for w in range(DVE_QUADS, GROUPS * QUADS):
        g, q = divmod(w, QUADS)
        ahead = min(NEAR + max(0, w - RAMP) * SLOPE, FAR)
        pairs = min(max(4 * q - 7.75, 0.25) ** 0.5 + ahead, PAIRS)
        need = int((g * PAIRS + pairs) * TILES * 2) + 2
        if w >= 30:
            need = max(need, int(PACE * w + START_PACE))
        need = min(need, total)
        steps += [("gather", x) for x in range(done, need)]
        done = max(done, need)
        steps.append(("wl", w))
    return steps


STAGE_TILES = 4
UNIT = STAGE_TILES * 2


def build(nc, ids, tables, dense_t, w_blocks, w1, b1, w2, b2, w3, y):
    fp32, fp32r, i32 = mybir.dt.float32, mybir.dt.float32r, mybir.dt.int32
    ALU = mybir.AluOpType
    ACT = mybir.ActivationFunctionType
    emb = nc.dram_tensor("emb_scratch", [GROUPS, PAIRS, GB, P128], fp32, kind="Internal").ap()

    ctx = ExitStack()
    with ctx:
        def sb(name, shape, dt=fp32):
            return ctx.enter_context(nc.sbuf_tensor(name, shape, dt))

        def sem(name):
            return ctx.enter_context(nc.semaphore(name))

        V = sb("V", [P128, PAIRS, GB])
        dup = sb("dup", [P128, 2, GB])
        hl = sb("hl", [P128, 2, GB], fp32r)
        wf = sb("wf", [P128, WF_SLOTS, LOAD_BLOCKS * W_COLS])
        wh = sb("wh", [P128, WQ_SLOTS, 4 * W_COLS], fp32r)
        wl = sb("wl", [P128, WQ_SLOTS, 4 * W_COLS], fp32r)
        P = sb("P", [P128, P_SLOTS, GB])
        z = sb("z", [P128, ZT, GB])
        w2s = sb("w2s", [P128, N1 // P128, N2])
        w3s = sb("w3s", [P128, N2 // P128])
        b1s = sb("b1s", [P128, N1 // P128])
        b2s = sb("b2s", [P128, N2 // P128])
        stage = sb("stage", [P128, 2, STAGE_TILES, P128])
        nat = sb("nat", [P128, TILES, P128])
        idx = sb("idx", [P128, GROUPS * TILES, F], i32)
        ident = sb("ident", [P128, P128])
        sel = sb("sel", [P128, 62])

        def w1_in(g):
            k = mlp_slot(g, "w1", 0)
            return P[:, k:k + 4, :].rearrange("p s b -> p (s b)")[:, 0:ZT * N1].rearrange("p (t n) -> p t n", t=ZT)

        Ups = ctx.enter_context(nc.psum_tensor("Ups", [P128, U_SLOTS, GB], fp32))
        Zps = ctx.enter_context(nc.psum_tensor("Zps", [P128, GB], fp32))

        consts_loaded = sem("consts_loaded")
        idx_loaded = sem("idx_loaded")
        ident_zeroed = sem("ident_zeroed")
        ident_ready = sem("ident_ready")
        sel_zeroed = sem("sel_zeroed")
        sel_ready = sem("sel_ready")
        gathered = [sem("gathered0"), sem("gathered1")]
        direct_gathered = [sem(f"direct_gathered{n}") for n in range(4)]
        emb_written = [sem("emb_written0"), sem("emb_written1")]
        nat_loaded = sem("nat_loaded")
        dup_loaded = [sem("dup_loaded0"), sem("dup_loaded1")]
        wf_loaded = [sem("wf_loaded0"), sem("wf_loaded1")]
        w1_loaded = sem("w1_loaded")
        dense_loaded = sem("dense_loaded")
        tr_done = sem("tr_done")
        main_done = sem("main_done")
        red_done = sem("red_done")
        mlp_done = sem("mlp_done")
        mul_done = sem("mul_done")
        lo_done = sem("lo_done")
        v_done = sem("v_done")
        hi_done = sem("hi_done")
        wh_done = sem("wh_done")
        z_done = sem("z_done")
        mlp_out = sem("mlp_out")
        wl_done = sem("wl_done")
        y_written = sem("y_written")

        block = ctx.enter_context(nc.Block())

        def wait(eng, s, value):
            if value > 0:
                eng.wait_ge(s, value)

        @block.sync
        def _(sp):
            sp.dma_start(idx[:, :, :], ids).then_inc(idx_loaded, 16)
            for kind, g, x in sp_order():
                if (kind, g, x) == ("w", 0, 5):
                    for dst, src in (
                        (w2s[:, :, :], w2.rearrange("(k p) n -> p k n", p=P128)),
                        (w3s[:, :], w3),
                        (b1s[:, :], b1),
                        (b2s[:, :], b2),
                    ):
                        sp.dma_start(dst, src).then_inc(consts_loaded, 16)
                if kind == "w":
                    c = g * (NB // LOAD_BLOCKS) + x
                    wait(sp, wl_done, 2 * (c - 1))
                    wait(sp, wh_done, 2 * (c - 1))
                    for h in range(2):
                        sp.dma_start(wf[D * h:D * h + D, c % WF_SLOTS, :],
                                     w_blocks[:, x * LOAD_BLOCKS * W_COLS:(x + 1) * LOAD_BLOCKS * W_COLS]
                                     ).then_inc(wf_loaded[c % WF_SLOTS], 16)
                elif kind == "w1":
                    sp.wait_ge(red_done, g * QUADS + QUADS - 2)
                    sp.dma_start(w1_in(g), w1).then_inc(w1_loaded, 16)
                elif kind == "nat":
                    m = g * PAIRS + x
                    wait(sp, tr_done, m)
                    wait(sp, emb_written[0], 16 * (m - DIRECT + 1))
                    wait(sp, emb_written[1], 16 * (m - DIRECT + 1))
                    sp.dma_start(nat[:, :, :], emb[g, x].rearrange("(t p) c -> p t c", p=P128)
                                 ).then_inc(nat_loaded, 16)
                else:
                    s = field_seq(g, x)
                    wait(sp, lo_done, s - 1)
                    wait(sp, v_done, g * PAIRS + PAIRS - x // 2)
                    for h in range(2):
                        sp.dma_start(dup[D * h:D * h + D, s % 2, :],
                                     V[D * (x % 2):D * (x % 2) + D, x // 2, :]).then_inc(dup_loaded[s % 2], 16)
            sp.wait_ge(y_written, 16 * GROUPS)

        @block.gpsimd
        def _(pool):
            pool.memset(ident[:, :], 0.0).then_inc(ident_zeroed, 1)
            pool.wait_ge(ident_zeroed, 1)
            pool.affine_select(out=ident[:, :], in_=ident[:, :], compare_op=ALU.not_equal, fill=1.0, base=0,
                               pattern=[[-1, P128]], channel_multiplier=1).then_inc(ident_ready, 1)
            pool.wait_ge(idx_loaded, 16)
            n_units = GROUPS * PAIRS * 2

            def write_out(u):
                g, rest = divmod(u, PAIRS * 2)
                r, h = divmod(rest, 2)
                pool.wait_ge(gathered[u % 2], 16 * UNIT * (u // 2 - DIRECT + 1))
                rows = slice(h * STAGE_TILES * P128, (h + 1) * STAGE_TILES * P128)
                pool.dma_start(emb[g, r, rows, :].rearrange("(t p) c -> p t c", p=P128), stage[:, u % 2, :, :]
                               ).then_inc(emb_written[u % 2], 16)

            for kind, x in pool_order():
                if kind == "gather":
                    u, k = divmod(x, UNIT)
                    g, rest = divmod(u, PAIRS * 2)
                    r, h = divmod(rest, 2)
                    t, f = k // 2, k % 2
                    direct = g == 0 and r < DIRECT
                    done = direct_gathered[u % 4] if direct else gathered[u % 2]
                    buf = nat[:, h * STAGE_TILES + t, :] if direct and r % 2 else stage[:, u % 2, t, :]
                    if k == 0 and h == 0 and direct and r >= 2:
                        pool.wait_ge(tr_done, r - 1)
                    if k == 0 and h == 0 and g == 0 and r == DIRECT:
                        pool.wait_ge(tr_done, DIRECT - 1)
                    if k == 0 and u >= 2 * DIRECT + 2:
                        pool.wait_ge(emb_written[u % 2], 16 * (u // 2 - DIRECT))
                    field = 2 * (PAIRS - 1 - r) + f
                    tile = g * TILES + h * STAGE_TILES + t
                    pool.indirect_dma_start(
                        out=buf[:, D * f:D * f + D], out_offset=None, in_=tables[field][:, :],
                        in_offset=bass.IndirectOffsetOnAxis(ap=idx[:, tile, field:field + 1], axis=0),
                    ).then_inc(done, 16)
                    if k == 1 and u > 2 * DIRECT:
                        write_out(u - 1)
                    if u == n_units - 1 and k == UNIT - 1:
                        write_out(u)
                else:
                    c = x // 2
                    if x == DVE_QUADS:
                        pool.wait_ge(wl_done, DVE_QUADS)
                    pool.wait_ge(wf_loaded[c % WF_SLOTS], 32 * (c // WF_SLOTS + 1))
                    pool.wait_ge(wh_done, x + 1)
                    wait(pool, main_done, 4 * (x - WQ_SLOTS + 1))
                    half = slice((x % 2) * 4 * W_COLS, (x % 2 + 1) * 4 * W_COLS)
                    pool.tensor_tensor(wl[:, x % WQ_SLOTS, :], wf[:, c % WF_SLOTS, half], wh[:, x % WQ_SLOTS, :],
                                       ALU.subtract).then_inc(wl_done, 1)

        @block.scalar
        def _(act):
            for kind, g, x in act_order():
                if kind == "v":
                    slot = U_AT[("tr", g, x)] % U_SLOTS
                    act.wait_ge(tr_done, g * PAIRS + x + 1)
                    if g:
                        act.wait_ge(mul_done, (g - 1) * NB + NB - PAIRS + x + 1)
                    act.copy(V[:, PAIRS - 1 - x, :], Ups[:, slot, :]).then_inc(v_done, 1)
                elif kind == "hi":
                    s = field_seq(g, x)
                    act.wait_ge(dup_loaded[s % 2], 32 * (s // 2 + 1))
                    if s >= 2:
                        g2, f2 = divmod(s - 2, FIELDS)
                        f2 = FIELDS - 1 - f2
                        act.wait_ge(main_done, g2 * NB + START[f2] + COUNT[f2])
                    act.copy(hl[:, s % 2, :], dup[:, s % 2, :]).then_inc(hi_done, 1)
                elif kind == "wh":
                    w = g * QUADS + x
                    c = w // 2
                    act.wait_ge(wf_loaded[c % WF_SLOTS], 32 * (c // WF_SLOTS + 1))
                    wait(act, main_done, 4 * (w - WQ_SLOTS + 1))
                    wait(act, wl_done, w - WQ_SLOTS + 1)
                    half = slice((w % 2) * 4 * W_COLS, (w % 2 + 1) * 4 * W_COLS)
                    act.copy(wh[:, w % WQ_SLOTS, :], wf[:, c % WF_SLOTS, half]).then_inc(wh_done, 1)
                elif kind == "z":
                    act.wait_ge(red_done, g * QUADS + min(ZQ * (x + 1), QUADS))
                    act.copy(z[:, x, :], Zps[:, :]).then_inc(z_done, 1)
                    if x == ZT - 1:
                        act.wait_ge(z_done, (g + 1) * ZT)
                        act.dma_start(z[DENSE_ROW:DENSE_ROW + DENSE, x, :],
                                      dense_t[:, g * GB:(g + 1) * GB]).then_inc(dense_loaded, 16)
                else:
                    slot = U_AT[("mlp", g, x)] % U_SLOTS
                    if g == 0 and x == 0:
                        act.wait_ge(consts_loaded, 16 * 4)
                    act.wait_ge(mlp_done, g * MLP_STEPS + x + 1)
                    if x < 4:
                        act.activation(P[:, mlp_slot(g, "h1", x), :], Ups[:, slot, :], ACT.Relu, bias=b1s[:, x:x + 1]
                                       ).then_inc(mlp_out, 1)
                    elif x < 6:
                        act.activation(P[:, mlp_slot(g, "h2", x - 4), :], Ups[:, slot, :], ACT.Relu, bias=b2s[:, x - 4:x - 3]
                                       ).then_inc(mlp_out, 1)
                    else:
                        act.copy(P[0:1, mlp_slot(g, "h2", 2), :], Ups[0:1, slot, :]).then_inc(mlp_out, 1)
                        act.wait_ge(mlp_out, (g + 1) * MLP_STEPS)
                        act.dma_start(y[g * GB:(g + 1) * GB, :].rearrange("n o -> o n"), P[0:1, mlp_slot(g, "h2", 2), :]
                                      ).then_inc(y_written, 16)

        @block.vector
        def _(dve):
            dve.memset(sel[:, :], 0.0).then_inc(sel_zeroed, 1)
            dve.wait_ge(sel_zeroed, 1)
            dve.memset(sel[0:D, 30:31], 1.0).then_inc(sel_ready, 1)
            dve.memset(sel[D:P128, 31:32], 1.0).then_inc(sel_ready, 1)
            for kind, g, x in dve_order():
                if kind == "mul":
                    n = g * NB + x
                    slot = U_AT[("main", g, x)] % U_SLOTS
                    dve.wait_ge(main_done, n + 1)
                    dve.wait_ge(v_done, g * PAIRS + PAIRS - BLOCKS[x][1])
                    wait(dve, red_done, (n - P_SLOTS) // 4 + 1)
                    if g and x < P_SLOTS:
                        dve.wait_ge(mlp_done, MLP_STEPS * (g - 1) + (4, 6, 7)[x // 4])
                        if x >= 8:
                            dve.wait_ge(y_written, 16 * g)
                    dve.tensor_tensor(P[:, n % P_SLOTS, :], Ups[:, slot, :], V[:, BLOCKS[x][1], :], ALU.mult
                                      ).then_inc(mul_done, 1)
                elif kind == "wl":
                    c = x // 2
                    dve.wait_ge(wf_loaded[c % WF_SLOTS], 32 * (c // WF_SLOTS + 1))
                    dve.wait_ge(wh_done, x + 1)
                    wait(dve, main_done, 4 * (x - WQ_SLOTS + 1))
                    half = slice((x % 2) * 4 * W_COLS, (x % 2 + 1) * 4 * W_COLS)
                    dve.tensor_tensor(wl[:, x % WQ_SLOTS, :], wf[:, c % WF_SLOTS, half], wh[:, x % WQ_SLOTS, :],
                                      ALU.subtract).then_inc(wl_done, 1)
                else:
                    s = field_seq(g, x)
                    dve.wait_ge(hi_done, s + 1)
                    dve.tensor_tensor(hl[D:P128, s % 2, :], dup[D:P128, s % 2, :], hl[D:P128, s % 2, :], ALU.subtract
                                      ).then_inc(lo_done, 1)

        @block.tensor
        def _(pe):
            pe.wait_ge(ident_ready, 1)
            pe.wait_ge(sel_ready, 2)

            def wait_slot(step):
                k = U_AT[step] - U_SLOTS
                if k < 0:
                    return
                kind, g, x = U_USES[k]
                if kind == "main":
                    pe.wait_ge(mul_done, g * NB + x + 1)
                elif kind == "tr":
                    pe.wait_ge(v_done, g * PAIRS + x + 1)
                else:
                    pe.wait_ge(mlp_out, g * MLP_STEPS + x + 1)

            for step in PE_STEPS:
                kind, g, x = step
                if kind == "early":
                    step = ("mlp", g, 0)
                if kind != "red":
                    if kind == "early" or step[::2] != ("mlp", 0):
                        wait_slot(step)
                    slot = U_AT[step] % U_SLOTS
                if kind == "tr":
                    m = g * PAIRS + x
                    direct = g == 0 and x < DIRECT
                    if not direct:
                        pe.wait_ge(nat_loaded, 16 * (m - DIRECT + 1))
                    for t in range(TILES):
                        rows = nat[:, t, :]
                        if direct and t % STAGE_TILES == 0:
                            pe.wait_ge(direct_gathered[2 * (x % 2) + t // STAGE_TILES], 16 * UNIT * (x // 2 + 1))
                        if direct and x % 2 == 0:
                            rows = stage[:, t // STAGE_TILES, t % STAGE_TILES, :]
                        last = pe.transpose(Ups[:, slot, P128 * t:P128 * (t + 1)], rows, ident[:, :])
                    last.then_inc(tr_done, 1)
                elif kind == "main":
                    i = BLOCKS[x][0]
                    w, s = g * QUADS + x // 4, field_seq(g, i)
                    pe.wait_ge(wh_done, w + 1)
                    pe.wait_ge(wl_done, w + 1)
                    pe.wait_ge(lo_done, s + 1)
                    cols = slice((x % 4) * W_COLS, (x % 4 + 1) * W_COLS)
                    for c in range(CHUNKS):
                        out = Ups[:, slot, HALF * c:HALF * (c + 1)]
                        v = hl[:, s % 2, HALF * c:HALF * (c + 1)]
                        pe.matmul(out, wh[:, w % WQ_SLOTS, cols], v, start=True, stop=False)
                        last = pe.matmul(out, wl[:, w % WQ_SLOTS, cols], v, start=False, stop=True)
                    last.then_inc(main_done, 1)
                elif kind == "red":
                    q = x % ZQ
                    pe.wait_ge(mul_done, g * NB + 4 * x + 4)
                    if q == 0:
                        wait(pe, z_done, g * ZT + x // ZQ)
                    for c in range(CHUNKS):
                        for strip in range(4):
                            n = g * NB + 4 * x + strip
                            last = pe.matmul(Zps[32 * strip:32 * strip + 32, HALF * c:HALF * (c + 1)],
                                             sel[:, 30 - 2 * q:62 - 2 * q],
                                             P[:, n % P_SLOTS, HALF * c:HALF * (c + 1)],
                                             start=q == 0, stop=q == ZQ - 1 or x == QUADS - 1)
                    last.then_inc(red_done, 1)
                elif kind == "early" or x < 4:
                    if kind == "early":
                        pe.wait_ge(consts_loaded, 16 * 4)
                        pe.wait_ge(w1_loaded, 16 * (g + 1))
                        pe.wait_ge(z_done, g * ZT + ZT - 1)
                    parts = [(c, k) for c in range(CHUNKS) for k in range(ZT)]
                    if kind == "early":
                        parts = parts[:ZT - 1]
                    elif x == 0:
                        parts = parts[ZT:-1] + [(0, ZT - 1), (1, ZT - 1)]
                    for c, k in parts:
                        if x == 0 and (c, k) == (0, ZT - 1):
                            pe.wait_ge(z_done, g * ZT + ZT)
                            pe.wait_ge(dense_loaded, 16 * (g + 1))
                        last = pe.matmul(Ups[:, slot, HALF * c:HALF * (c + 1)],
                                         w1_in(g)[:, k, P128 * x:P128 * (x + 1)], z[:, k, HALF * c:HALF * (c + 1)],
                                         start=k == 0, stop=k == ZT - 1)
                    if kind == "mlp":
                        last.then_inc(mlp_done, 1)
                elif x < 6:
                    m = x - 4
                    for c in range(CHUNKS):
                        for k in range(4):
                            if x == 4 and c == 0:
                                pe.wait_ge(mlp_out, g * MLP_STEPS + k + 1)
                            last = pe.matmul(Ups[:, slot, HALF * c:HALF * (c + 1)],
                                             w2s[:, k, P128 * m:P128 * (m + 1)],
                                             P[:, mlp_slot(g, "h1", k), HALF * c:HALF * (c + 1)],
                                             start=k == 0, stop=k == 3)
                    last.then_inc(mlp_done, 1)
                else:
                    for c in range(CHUNKS):
                        for k in range(2):
                            if c == 0:
                                pe.wait_ge(mlp_out, g * MLP_STEPS + 5 + k)
                            last = pe.matmul(Ups[0:1, slot, HALF * c:HALF * (c + 1)], w3s[:, k:k + 1],
                                             P[:, mlp_slot(g, "h2", k), HALF * c:HALF * (c + 1)], start=k == 0, stop=k == 1)
                    last.then_inc(mlp_done, 1)


def kernel(**inputs):
    import concourse.bacc as bacc
    from concourse.bass_utils import run_bass_kernel_spmd

    W = np.asarray(inputs["L0_rec_W"])
    first = {}
    for i in range(F):
        first[i] = sum(F - 1 - a for a in range(i))
    wb = np.zeros((D, NB, 2, D), W.dtype)
    for n, (i, jp) in enumerate(BLOCKS):
        for half in range(2):
            j = 2 * jp + half
            if j > i:
                wb[:, n, half, :] = W[first[i] + j - i - 1]
    W1 = np.asarray(inputs["W_top1"])
    w1 = np.zeros((P128, ZT, N1), W1.dtype)
    for n, (i, jp) in enumerate(BLOCKS):
        for half in range(2):
            j = 2 * jp + half
            if j > i:
                row, tile = z_place(n, half)
                w1[row, tile] = W1[first[i] + j - i - 1]
    pairs = F * (F - 1) // 2
    w1[DENSE_ROW:DENSE_ROW + DENSE, ZT - 1] = W1[pairs:]
    arrays = {
        "ids": np.ascontiguousarray(np.asarray(inputs["ids"]).reshape(B // P128, P128, F).transpose(1, 0, 2)),
        "dense_t": np.ascontiguousarray(np.asarray(inputs["dense_ctx"]).T),
        "w_blocks": wb.reshape(D, NB * W_COLS),
        "w1": w1,
        "b1": np.ascontiguousarray(np.asarray(inputs["b_top1"]).reshape(-1, P128).T),
        "w2": np.ascontiguousarray(inputs["W_top2"]),
        "b2": np.ascontiguousarray(np.asarray(inputs["b_top2"]).reshape(-1, P128).T),
        "w3": np.ascontiguousarray(np.asarray(inputs["W_top3"]).reshape(-1, P128).T),
    }
    for f in range(F):
        arrays[f"tbl_{f}"] = np.ascontiguousarray(inputs[f"tbl_{f}"])
    nc = bacc.Bacc("TRN2", target_bir_lowering=False, num_devices=1)
    t = {k: nc.dram_tensor(k, a.shape, mybir.dt.from_np(a.dtype), kind="ExternalInput").ap()
         for k, a in arrays.items()}
    y = nc.dram_tensor("y", [B, 1], mybir.dt.float32, kind="ExternalOutput").ap()
    build(nc, t["ids"], [t[f"tbl_{f}"] for f in range(F)], t["dense_t"], t["w_blocks"], t["w1"], t["b1"],
          t["w2"], t["b2"], t["w3"], y)
    r = run_bass_kernel_spmd(nc, [arrays], core_ids=[0])
    return r.results[0]["y"]
```
